# Optimizing a Trainium2 kernel written in Bass

```python
import numpy as np
import jax
import jax.numpy as jnp

def _softmax(x, axis=-1):
    return jax.nn.softmax(x, axis=axis)

def _gelu(x):
    return jax.nn.gelu(x, approximate=True)

def _silu(x):
    return jax.nn.silu(x)

def _sigmoid(x):
    return jax.nn.sigmoid(x)

def _layernorm(x, axis=-1, eps=1e-05):
    m = jnp.mean(x, axis=axis, keepdims=True)
    v = jnp.var(x, axis=axis, keepdims=True)
    return (x - m) / jnp.sqrt(v + eps)

def _scatter_add(tgt, idx, src, axis=0):
    return tgt.at[idx].add(src)

def _segment_sum(src, seg, n):
    return jax.ops.segment_sum(src, seg, n)
kernel_name = 'mk_gnn_preln_d4_gnn_r32_91e867'

def setup_inputs(seed: int=0):
    np.random.seed(seed)
    _w = jnp.asarray

    def _rec_inputs():
        import jax
        import jax.numpy as jnp
        _gk = jax.random.key(seed)
        x = -0.0001006 + 1 * jax.random.normal(jax.random.fold_in(_gk, 1), (3125, 96), jnp.float32)
        src = jax.random.randint(jax.random.fold_in(_gk, 2), (100000,), 0, 3125, jnp.int32)
        dst = jnp.minimum((3125 * jax.random.uniform(jax.random.fold_in(_gk, 3), (100000,)) ** 2.0).astype(jnp.int32), 99999)
        _o = jnp.argsort(dst, stable=True)
        src = src[_o]
        dst = dst[_o]
        edge_attr_32 = 0.000196303 + 1.00016 * jax.random.normal(jax.random.fold_in(_gk, 11), (100000, 32), jnp.float32)
        edge_attr_96 = 5.93493e-05 + 1.00006 * jax.random.normal(jax.random.fold_in(_gk, 12), (100000, 96), jnp.float32)
        return (x, src, dst, edge_attr_32, edge_attr_96)
    x, src, dst, edge_attr_32, edge_attr_96 = _rec_inputs()

    def _L0_gnn_setup():
        import jax, jax.numpy as jnp
        import numpy as np
        K = 10
        ALPHA = 0.1
        BETA = 0.9
        N_NODES = 50000
        N_EDGES = 25000
        D_FEAT = 96
        key = jax.random.key(seed)
        k1, k2, k3 = jax.random.split(key, 3)
        x = jax.random.normal(k1, (N_NODES, D_FEAT), dtype=jnp.float32)
        row = jax.random.randint(k2, (N_EDGES,), 0, N_NODES, dtype=jnp.int64)
        col = jax.random.randint(k3, (N_EDGES,), 0, N_NODES, dtype=jnp.int64)
        edge_index = jnp.stack([row, col], axis=0)
        return {'x': x, 'edge_index': edge_index}
    _L0_gnn_all = _L0_gnn_setup()
    _L0_gnn_in = {k: v for k, v in _L0_gnn_all.items() if k in ()}
    del _L0_gnn_all

    def _L1_gnn_setup():
        import jax, jax.numpy as jnp
        import numpy as np
        N_NODES = 50000
        N_EDGES = 25000
        NUM_FEATURES = 96
        HIDDEN = 96

        def _glorot(key, fan_in, fan_out):
            s = np.sqrt(6.0 / (fan_in + fan_out)).astype(np.float32)
            return jax.random.uniform(key, (fan_in, fan_out), minval=-s, maxval=s, dtype=jnp.float32)

        def _gcn_conv(x, src, dst, W, b):
            n = x.shape[0]
            h = x @ W
            deg = jax.ops.segment_sum(jnp.ones_like(dst, dtype=h.dtype), dst, num_segments=n) + 1.0
            dinv = jax.lax.rsqrt(deg)
            norm = dinv[src] * dinv[dst]
            agg = jax.ops.segment_sum(h[src] * norm[:, None], dst, num_segments=n)
            return agg + h * (dinv * dinv)[:, None] + b
        key = jax.random.key(seed)
        ks = jax.random.split(key, 8)
        x = jax.random.normal(ks[0], (N_NODES, NUM_FEATURES), dtype=jnp.float32)
        edge_index = jax.random.randint(ks[1], (2, N_EDGES), 0, N_NODES, dtype=jnp.int64)
        return {'x': x, 'W1': _glorot(ks[2], NUM_FEATURES, HIDDEN), 'b1': jnp.zeros((HIDDEN,), jnp.float32), 'W2': _glorot(ks[3], HIDDEN, HIDDEN), 'b2': jnp.zeros((HIDDEN,), jnp.float32), 'W3': _glorot(ks[4], HIDDEN, HIDDEN), 'b3': jnp.zeros((HIDDEN,), jnp.float32), 'edge_index': edge_index}
    _L1_gnn_all = _L1_gnn_setup()
    _L1_gnn_in = {k: v for k, v in _L1_gnn_all.items() if k in ('W1', 'b1', 'W2', 'b2', 'W3', 'b3')}
    del _L1_gnn_all

    def _L2_gnn_setup():
        import jax, jax.numpy as jnp
        import numpy as np
        N_NODES = 50000
        N_EDGES = 25000
        DIM = 96
        key = jax.random.key(seed)
        k = jax.random.split(key, 6)
        x = jax.random.normal(k[0], (N_NODES, DIM), dtype=jnp.float32)
        edge_index = jax.random.randint(k[1], (2, N_EDGES), 0, N_NODES, dtype=jnp.int64)
        edge_attr = jax.random.normal(k[2], (N_EDGES, DIM), dtype=jnp.float32)
        scale = 1.0 / np.sqrt(DIM)
        W1 = jax.random.normal(k[3], (DIM, DIM), dtype=jnp.float32) * scale
        b1 = jnp.zeros((DIM,), dtype=jnp.float32)
        W2 = jax.random.normal(k[4], (DIM, DIM), dtype=jnp.float32) * scale
        b2 = jnp.zeros((DIM,), dtype=jnp.float32)
        return {'x': x, 'edge_index': edge_index, 'edge_attr': edge_attr, 'W1': W1, 'b1': b1, 'W2': W2, 'b2': b2}
    _L2_gnn_all = _L2_gnn_setup()
    _L2_gnn_in = {k: v for k, v in _L2_gnn_all.items() if k in ('W1', 'b1', 'W2', 'b2')}
    del _L2_gnn_all

    def _L3_gnn_setup():
        import jax, jax.numpy as jnp
        import numpy as np
        N, E = (50000, 25000)
        ND, ED = (96, 32)

        def _gelu(x):
            return jax.nn.gelu(x, approximate=False)
        key = jax.random.key(seed)
        ks = jax.random.split(key, 16)
        s = lambda fan_in: 1.0 / np.sqrt(fan_in)
        inp = {'x': jax.random.normal(ks[0], (N, ND), jnp.float32), 'edge_index': jax.random.randint(ks[1], (2, E), 0, N, jnp.int32), 'edge_attr': jax.random.normal(ks[2], (E, ED), jnp.float32), 'mW1': jax.random.uniform(ks[3], (ND + ED, ND), jnp.float32, -s(ND + ED), s(ND + ED)), 'mb1': jnp.zeros((ND,), jnp.float32), 'mW2': jax.random.uniform(ks[4], (ND, ND), jnp.float32, -s(ND), s(ND)), 'mb2': jnp.zeros((ND,), jnp.float32), 'gW1': jax.random.uniform(ks[5], (ND + ED, ND), jnp.float32, -s(ND + ED), s(ND + ED)), 'gb1': jnp.zeros((ND,), jnp.float32), 'gW2': jax.random.uniform(ks[6], (ND, 1), jnp.float32, -s(ND), s(ND)), 'gb2': jnp.zeros((1,), jnp.float32), 'uW1': jax.random.uniform(ks[7], (2 * ND, ND), jnp.float32, -s(2 * ND), s(2 * ND)), 'ub1': jnp.zeros((ND,), jnp.float32), 'uW2': jax.random.uniform(ks[8], (ND, ND), jnp.float32, -s(ND), s(ND)), 'ub2': jnp.zeros((ND,), jnp.float32), 'ln_g': jnp.ones((ND,), jnp.float32), 'ln_b': jnp.zeros((ND,), jnp.float32)}
        return inp
    _L3_gnn_all = _L3_gnn_setup()
    _L3_gnn_in = {k: v for k, v in _L3_gnn_all.items() if k in ('mW1', 'mb1', 'mW2', 'mb2', 'gW1', 'gb1', 'gW2', 'gb2', 'uW1', 'ub1', 'uW2', 'ub2', 'ln_g', 'ln_b')}
    del _L3_gnn_all
    return {'x': x, 'src': src, 'dst': dst, 'edge_attr_32': edge_attr_32, 'edge_attr_96': edge_attr_96, 'L1_gnn_W1': _L1_gnn_in['W1'], 'L1_gnn_b1': _L1_gnn_in['b1'], 'L1_gnn_W2': _L1_gnn_in['W2'], 'L1_gnn_b2': _L1_gnn_in['b2'], 'L1_gnn_W3': _L1_gnn_in['W3'], 'L1_gnn_b3': _L1_gnn_in['b3'], 'L2_gnn_W1': _L2_gnn_in['W1'], 'L2_gnn_b1': _L2_gnn_in['b1'], 'L2_gnn_W2': _L2_gnn_in['W2'], 'L2_gnn_b2': _L2_gnn_in['b2'], 'L3_gnn_mW1': _L3_gnn_in['mW1'], 'L3_gnn_mb1': _L3_gnn_in['mb1'], 'L3_gnn_mW2': _L3_gnn_in['mW2'], 'L3_gnn_mb2': _L3_gnn_in['mb2'], 'L3_gnn_gW1': _L3_gnn_in['gW1'], 'L3_gnn_gb1': _L3_gnn_in['gb1'], 'L3_gnn_gW2': _L3_gnn_in['gW2'], 'L3_gnn_gb2': _L3_gnn_in['gb2'], 'L3_gnn_uW1': _L3_gnn_in['uW1'], 'L3_gnn_ub1': _L3_gnn_in['ub1'], 'L3_gnn_uW2': _L3_gnn_in['uW2'], 'L3_gnn_ub2': _L3_gnn_in['ub2'], 'L3_gnn_ln_g': _L3_gnn_in['ln_g'], 'L3_gnn_ln_b': _L3_gnn_in['ln_b']}

def reference(x, src, dst, edge_attr_32, edge_attr_96, L1_gnn_W1, L1_gnn_b1, L1_gnn_W2, L1_gnn_b2, L1_gnn_W3, L1_gnn_b3, L2_gnn_W1, L2_gnn_b1, L2_gnn_W2, L2_gnn_b2, L3_gnn_mW1, L3_gnn_mb1, L3_gnn_mW2, L3_gnn_mb2, L3_gnn_gW1, L3_gnn_gb1, L3_gnn_gW2, L3_gnn_gb2, L3_gnn_uW1, L3_gnn_ub1, L3_gnn_uW2, L3_gnn_ub2, L3_gnn_ln_g, L3_gnn_ln_b):
    import jax
    import jax.numpy as jnp

    def _L0_gnn_ref(x, edge_index):
        import jax, jax.numpy as jnp
        import numpy as np
        K = 10
        ALPHA = 0.1
        BETA = 0.9
        N_NODES = 50000
        N_EDGES = 25000
        D_FEAT = 96
        n = x.shape[0]
        row, col = (edge_index[0], edge_index[1])
        ones = jnp.ones((edge_index.shape[1],), dtype=x.dtype)
        deg_row = jnp.maximum(jax.ops.segment_sum(ones, row, num_segments=n), 1.0)
        deg_col = jnp.maximum(jax.ops.segment_sum(ones, col, num_segments=n), 1.0)
        w = jax.lax.rsqrt(deg_row[row] * deg_col[col])

        def spmm(feat):
            msg = feat[col] * w[:, None]
            return jax.ops.segment_sum(msg, row, num_segments=n)
        h = x
        out = h
        for _ in range(K):
            out = spmm(out) * BETA + h * ALPHA
        theta = BETA ** K + ALPHA * sum((BETA ** i for i in range(K)))
        return out / jnp.asarray(theta, dtype=x.dtype)

    def _L1_gnn_ref(x, W1, b1, W2, b2, W3, b3, edge_index):
        import jax, jax.numpy as jnp
        import numpy as np
        N_NODES = 50000
        N_EDGES = 25000
        NUM_FEATURES = 96
        HIDDEN = 96

        def _glorot(key, fan_in, fan_out):
            s = np.sqrt(6.0 / (fan_in + fan_out)).astype(np.float32)
            return jax.random.uniform(key, (fan_in, fan_out), minval=-s, maxval=s, dtype=jnp.float32)

        def _gcn_conv(x, src, dst, W, b):
            n = x.shape[0]
            h = x @ W
            deg = jax.ops.segment_sum(jnp.ones_like(dst, dtype=h.dtype), dst, num_segments=n) + 1.0
            dinv = jax.lax.rsqrt(deg)
            norm = dinv[src] * dinv[dst]
            agg = jax.ops.segment_sum(h[src] * norm[:, None], dst, num_segments=n)
            return agg + h * (dinv * dinv)[:, None] + b
        src, dst = (edge_index[0], edge_index[1])
        h = jax.nn.relu(_gcn_conv(x, src, dst, W1, b1))
        h = jax.nn.relu(_gcn_conv(h, src, dst, W2, b2))
        return _gcn_conv(h, src, dst, W3, b3)

    def _L2_gnn_ref(x, edge_index, edge_attr, W1, b1, W2, b2):
        import jax, jax.numpy as jnp
        import numpy as np
        N_NODES = 50000
        N_EDGES = 25000
        DIM = 96
        src = edge_index[0]
        dst = edge_index[1]
        msg = jax.nn.relu(x[src] + edge_attr)
        aggr = jax.ops.segment_sum(msg, dst, num_segments=x.shape[0])
        h = x + aggr
        h = jax.nn.relu(h @ W1 + b1) @ W2 + b2
        return x + jax.nn.relu(h)

    def _L3_gnn_ref(x, edge_index, edge_attr, mW1, mb1, mW2, mb2, gW1, gb1, gW2, gb2, uW1, ub1, uW2, ub2, ln_g, ln_b):
        import jax, jax.numpy as jnp
        import numpy as np
        N, E = (50000, 25000)
        ND, ED = (96, 32)

        def _gelu(x):
            return jax.nn.gelu(x, approximate=False)
        src, dst = (edge_index[0], edge_index[1])
        edge_input = jnp.concatenate([x[src], edge_attr], axis=-1)
        messages = _gelu(edge_input @ mW1 + mb1) @ mW2 + mb2
        gates = jax.nn.sigmoid(_gelu(edge_input @ gW1 + gb1) @ gW2 + gb2)
        aggregated = jax.ops.segment_sum(messages * gates, dst, num_segments=x.shape[0])
        combined = jnp.concatenate([x, aggregated], axis=-1)
        update = _gelu(combined @ uW1 + ub1) @ uW2 + ub2
        h = x + update
        mu = jnp.mean(h, axis=-1, keepdims=True)
        var = jnp.mean(jnp.square(h - mu), axis=-1, keepdims=True)
        return (h - mu) * jax.lax.rsqrt(var + 1e-05) * ln_g + ln_b
    edge_index = jnp.stack([src, dst])
    h = jnp.maximum(_layernorm(x, axis=-1), 0.0)
    x = x + _L0_gnn_ref(h, edge_index)
    h = jnp.maximum(_layernorm(x, axis=-1), 0.0)
    x = x + _L1_gnn_ref(h, L1_gnn_W1, L1_gnn_b1, L1_gnn_W2, L1_gnn_b2, L1_gnn_W3, L1_gnn_b3, edge_index)
    h = jnp.maximum(_layernorm(x, axis=-1), 0.0)
    x = x + _L2_gnn_ref(h, edge_index, edge_attr_96, L2_gnn_W1, L2_gnn_b1, L2_gnn_W2, L2_gnn_b2)
    h = jnp.maximum(_layernorm(x, axis=-1), 0.0)
    x = x + _L3_gnn_ref(h, edge_index, edge_attr_32, L3_gnn_mW1, L3_gnn_mb1, L3_gnn_mW2, L3_gnn_mb2, L3_gnn_gW1, L3_gnn_gb1, L3_gnn_gW2, L3_gnn_gb2, L3_gnn_uW1, L3_gnn_ub1, L3_gnn_uW2, L3_gnn_ub2, L3_gnn_ln_g, L3_gnn_ln_b)
    return x

_drawn_inputs = setup_inputs


def setup_inputs(seed=0):
    import zlib

    import numpy as np

    out = dict(_drawn_inputs(seed))
    spreads = {'L1_gnn_b1': (0.0, 0.396),
     'L1_gnn_b2': (0.0, 0.1),
     'L1_gnn_b3': (0.0, 0.1),
     'L2_gnn_b1': (0.0, 2.0),
     'L2_gnn_b2': (0.0, 2.0),
     'L3_gnn_mb1': (0.0, 2.0),
     'L3_gnn_mb2': (0.0, 2.0),
     'L3_gnn_gb1': (0.0, 2.0),
     'L3_gnn_ub1': (0.0, 2.0),
     'L3_gnn_ub2': (0.0, 2.0),
     'L3_gnn_ln_g': (1.0, 0.6),
     'L3_gnn_ln_b': (0.0, 0.8)}
    factors = {'edge_attr_32': 8.0,
     'L3_gnn_mW1': 3.134,
     'L3_gnn_mW2': 2.917,
     'L3_gnn_gW1': 8.0,
     'L3_gnn_gW2': 22.192}
    for name, (base, spread) in spreads.items():
        noise = np.random.default_rng([zlib.crc32(name.encode()), seed]).standard_normal(out[name].shape)
        drawn = base * np.exp(spread * noise) if base else spread * noise
        out[name] = jnp.asarray(drawn.astype(out[name].dtype))
    for name, factor in factors.items():
        out[name] = (out[name] * factor).astype(out[name].dtype)
    return out
```

```python
import concourse.bass as bass
from concourse import mybir
from contextlib import ExitStack

N = 3125
D = 96
DE = 32
E = 100000
NP = 125
NT = N // NP
EP = 128
GT = 8
NG = 98
ET = NG * GT
SUB = 4
NPAIR = ET // 2
CW = N + 3
BANK = 512
MID = 1562
HOPS = 10
ALPHA = 0.1
BETA = 0.9
THETA = BETA ** HOPS + ALPHA * sum(BETA ** i for i in range(HOPS))
LIFT = 64.0
EPS = 1e-5
LOADS = 19
FAR = 8192.0
GROUPS = [(m, min(4, NT - m)) for m in range(0, NT, 4)]

F32 = mybir.dt.float32
F16 = mybir.dt.float16
BF16 = mybir.dt.bfloat16
I32 = mybir.dt.int32
ALU = mybir.AluOpType
ACT = mybir.ActivationFunctionType
AX = mybir.AxisListType.X


def spread(ap, n):
    return ap.unsqueeze(2).to_broadcast([ap.shape[0], ap.shape[1], n])


def within(nc, value, most):
    return nc.s_assert_within(value, 0, most, skip_runtime_bounds_check_because=
                              "the tables that the bounds are read from hold it in this range for any edges")


class Chain:

    def __init__(self, engine, sem):
        self.engine, self.sem, self.count = engine, sem, 0

    def __call__(self, instruction):
        self.count += 1
        instruction.then_inc(self.sem, 1)
        self.engine.wait_ge(self.sem, self.count)


def inverse_root(nc, link, act_in, act_out, dve, value, root, inv, tmp, nth):
    dve.sem_inc(act_in, 1)
    dve.wait_ge(act_out, nth)
    link(nc.vector.reciprocal(inv, root))
    link(nc.vector.tensor_tensor(tmp, inv, inv, ALU.mult))
    link(nc.vector.tensor_tensor(tmp, tmp, value, ALU.mult))
    link(nc.vector.tensor_scalar(tmp, tmp, -0.5, 1.5, ALU.mult, ALU.add))
    link(nc.vector.tensor_tensor(inv, inv, tmp, ALU.mult))


def normalize_relu(nc, link, act_in, act_out, dve, x, h, square, s, nth, relu=True):
    mean, var, root, inv, tmp = (s[:, i, :] for i in range(5))
    link(nc.vector.reduce_sum(mean, x, AX))
    link(nc.vector.tensor_scalar(mean, mean, 1.0 / D, None, ALU.mult))
    link(nc.vector.tensor_tensor(h, x, spread(mean, D), ALU.subtract))
    link(nc.vector.tensor_tensor(square, h, h, ALU.mult))
    link(nc.vector.reduce_sum(var, square, AX))
    link(nc.vector.tensor_scalar(var, var, 1.0 / D, EPS, ALU.mult, ALU.add))
    inverse_root(nc, link, act_in, act_out, dve, var, root, inv, tmp, nth)
    if relu:
        link(nc.vector.scalar_tensor_tensor(out=h, in0=h, scalar=0.0, in1=spread(inv, D),
                                            op0=ALU.max, op1=ALU.mult))
    else:
        link(nc.vector.tensor_tensor(h, h, spread(inv, D), ALU.mult))


class Memory:

    def __init__(self, nc, ctx, stage):
        self.nc, self.ctx, self.stage = nc, ctx, stage

    def sb(self, name, shape, dt):
        return self.ctx.enter_context(self.nc.sbuf_tensor(f"{self.stage}_{name}", shape, dt))

    def ps(self, name, shape, dt):
        return self.ctx.enter_context(self.nc.psum_tensor(f"{self.stage}_{name}", shape, dt))

    def sem(self, name):
        return self.ctx.enter_context(self.nc.semaphore(f"{self.stage}_{name}"))


def count_edges(nc, g, x, src, dst, dst_groups):
    with ExitStack() as ctx:
        m = Memory(nc, ctx, "cnt")
        work = g["work"]
        iota = work[:, 0:CW]
        onehot = [work[:, CW * (i + 1):CW * (i + 2)] for i in range(2)]
        pick = m.sb("pick", [EP, 2, 128], F16)
        dst_i = m.sb("dst_i", [EP, ET], I32)
        src_i = m.sb("src_i", [EP, ET], I32)
        dst_f = m.sb("dst_f", [EP, ET], F32)
        zeros = m.sb("zeros", [128, BANK], F16)
        src_f = m.sb("src_f", [EP, ET], F32)
        low = g["counts"][:, :].bitcast(F32)
        groups_i = low[:NG, 0:1024].bitcast(I32)
        groups_f = low[:NG, 1024:2048]
        pmin = low[:NG, 2048:2052]
        pmax = low[:NG, 2052:2056]
        first = low[:NG, 2060:2085]
        last = low[:NG, 2085:2110]
        pair_no = low[:NG, 2110:2114]
        in_lo = low[:NG, 2200:2300].rearrange("p (j c) -> p j c", c=4)
        in_hi = low[:NG, 2300:2400].rearrange("p (j c) -> p j c", c=4)
        lo_part = low[:NG, 2400:2425]
        hi_part = low[:NG, 2425:2450]
        span = low[:NT, 2450:2453]
        gmin = low[:NG, 2460:2462]
        gmax = low[:NG, 2462:2464]
        step_at = low[:NG, 2464:2488]
        over = low[:NG, 2500:2548].rearrange("p (a j) -> p a j", a=2)
        jlo = low[:NG, 2550:2552]
        jcount = low[:NG, 2552:2554]
        jtotal = low[:NG, 2554:2555]
        before = low[:, 2600:2728]
        table_ps = m.ps("table_ps", [128, BANK], F32)
        sums = m.ps("sums", [128, 7 * BANK], F32)
        deg7 = m.sb("deg7", [NP, NT, 7], F32)
        loaded = m.sem("loaded"); made = m.sem("made"); chain = m.sem("chain")
        root_asked = m.sem("root_asked"); root_done = m.sem("root_done")
        parts = m.sem("parts"); turned = m.sem("turned"); spans = m.sem("spans"); rows = m.sem("rows")
        tables = m.sem("tables"); placed = m.sem("placed")
        ready = [m.sem(f"ready{i}") for i in range(2)]
        used = [m.sem(f"used{i}") for i in range(2)]
        emptied = [m.sem(f"emptied{b}") for b in range(7)]
        ident = g["ident"]
        widths = [min(BANK, N - BANK * b) for b in range(7)]
        block = ctx.enter_context(nc.Block())

        @block.sync
        def _(sp):
            sp.dma_start(groups_i, dst_groups).then_inc(loaded, 16)
            sp.dma_start(src_i[:, :], src).then_inc(loaded, 16)
            sp.dma_start(dst_i[:, :], dst).then_inc(loaded, 16)
            sp.dma_start(g["x"][:, :, :], x.rearrange("(t p) d -> p t d", p=NP)).then_inc(loaded, 16)

        @block.gpsimd
        def _(pool):
            nc.gpsimd.iota(iota, [[1, CW]], base=-MID, channel_multiplier=0,
                           allow_small_or_imprecise_dtypes=True).then_inc(made, 1)
            nc.gpsimd.iota(first, [[NP, NT]], base=0, channel_multiplier=0,
                           allow_small_or_imprecise_dtypes=True).then_inc(made, 1)
            nc.gpsimd.iota(last, [[NP, NT]], base=NP - 1, channel_multiplier=0,
                           allow_small_or_imprecise_dtypes=True).then_inc(made, 1)
            nc.gpsimd.iota(step_at, [[NP, NT - 1]], base=NP, channel_multiplier=0,
                           allow_small_or_imprecise_dtypes=True).then_inc(made, 1)
            nc.gpsimd.iota(pair_no, [[1, 4]], base=0, channel_multiplier=4,
                           allow_small_or_imprecise_dtypes=True).then_inc(made, 1)
            nc.gpsimd.memset(ident[:, :], 0.0).then_inc(placed, 1)
            nc.gpsimd.memset(before, 1.0).then_inc(placed, 1)
            nc.gpsimd.memset(zeros[:, :], 0.0).then_inc(made, 1)
            pool.wait_ge(placed, 2)
            nc.gpsimd.affine_select(out=ident[:, :], in_=ident[:, :], compare_op=ALU.not_equal, fill=1.0,
                                    base=0, pattern=[[-1, 128]], channel_multiplier=1).then_inc(made, 1)
            nc.gpsimd.affine_select(out=before, in_=before, compare_op=ALU.is_gt, fill=0.0,
                                    base=0, pattern=[[1, 128]], channel_multiplier=-1).then_inc(made, 1)

        @block.scalar
        def _(act):
            act.wait_ge(tables, 1)
            with act.Fori(0, NT) as j:
                end = act.value_load(g["pairs"][0:1, bass.ds(j + 1, 1)], min_val=1, max_val=NT * NPAIR)
                act.wait_ge(used[1], end + 1)
                for b in range(7):
                    w = widths[b]
                    nc.scalar.activation(g["counts"][0:NP, bass.ds(j * CW + BANK * b, w)],
                                         sums[0:NP, BANK * b:BANK * b + w], ACT.Copy,
                                         accum_out=deg7[:, bass.ds(j, 1), b:b + 1].rearrange("p a b -> p (a b)"),
                                         ).then_inc(emptied[b], 1)
            act.wait_ge(root_asked, 1)
            nc.scalar.activation(g["s"][:, 2, :], g["s"][:, 1, :], ACT.Sqrt).then_inc(root_done, 1)

        @block.vector
        def _(dve):
            link = Chain(dve, chain)
            dve.wait_ge(loaded, 64)
            dve.wait_ge(made, 8)
            link(nc.vector.tensor_copy(groups_f, groups_i))
            by_pair = groups_f.rearrange("p (c e) -> p c e", c=4)
            link(nc.vector.tensor_reduce(pmin, by_pair, AX, ALU.min))
            link(nc.vector.tensor_reduce(pmax, by_pair, AX, ALU.max))
            wide = [NG, NT, 4]
            mins = pmin.unsqueeze(1).to_broadcast(wide)
            maxs = pmax.unsqueeze(1).to_broadcast(wide)
            link(nc.vector.tensor_tensor(in_lo, mins, spread(last, 4), ALU.is_le))
            link(nc.vector.tensor_tensor(in_hi, maxs, spread(first, 4), ALU.is_ge))
            link(nc.vector.tensor_tensor(in_lo, in_lo, in_hi, ALU.mult))
            link(nc.vector.tensor_copy(in_hi, in_lo))
            link(nc.vector.tensor_scalar(pair_no, pair_no, 1.0, None, ALU.add))
            numbers = pair_no.unsqueeze(1).to_broadcast(wide)
            link(nc.vector.tensor_tensor(in_hi, in_hi, numbers, ALU.mult))
            link(nc.vector.tensor_scalar(pair_no, pair_no, -(FAR + 1.0), None, ALU.add))
            link(nc.vector.tensor_tensor(in_lo, in_lo, numbers, ALU.mult))
            link(nc.vector.tensor_reduce(lo_part, in_lo, AX, ALU.min))
            nc.vector.tensor_reduce(hi_part, in_hi, AX, ALU.max).then_inc(parts, 1)
            dve.wait_ge(turned, 1)
            link(nc.vector.tensor_reduce(span[:, 0:1], table_ps[0:NT, 0:NG], AX, ALU.min))
            link(nc.vector.tensor_reduce(span[:, 1:2], table_ps[0:NT, 128:128 + NG], AX, ALU.max))
            link(nc.vector.tensor_scalar(span[:, 1:2], span[:, 1:2], 1.0, None, ALU.max))
            link(nc.vector.tensor_scalar(span[:, 0:1], span[:, 0:1], FAR, None, ALU.add))
            link(nc.vector.tensor_scalar(span[:, 2:3], span[:, 1:2], -1.0, None, ALU.add))
            link(nc.vector.tensor_tensor(span[:, 0:1], span[:, 0:1], span[:, 2:3], ALU.min))
            link(nc.vector.tensor_tensor(span[:, 1:2], span[:, 1:2], span[:, 0:1], ALU.subtract))
            link(nc.vector.tensor_reduce(gmin, pmin.rearrange("p (a b) -> p a b", b=2), AX, ALU.min))
            link(nc.vector.tensor_reduce(gmax, pmax.rearrange("p (a b) -> p a b", b=2), AX, ALU.max))
            steps = step_at.unsqueeze(1).to_broadcast([NG, 2, NT - 1])
            link(nc.vector.tensor_tensor(over, spread(gmin, NT - 1), steps, ALU.is_ge))
            link(nc.vector.reduce_sum(jlo, over, AX))
            link(nc.vector.tensor_tensor(over, spread(gmax, NT - 1), steps, ALU.is_ge))
            link(nc.vector.reduce_sum(jcount, over, AX))
            link(nc.vector.tensor_tensor(jcount, jcount, jlo, ALU.subtract))
            link(nc.vector.tensor_scalar(jcount, jcount, 1.0, None, ALU.add))
            nc.vector.reduce_sum(jtotal, jcount, AX).then_inc(spans, 1)
            dve.wait_ge(rows, 1)
            nc.vector.tensor_copy(g["pairs"][:, :], table_ps[0:1, 0:NT + 1])
            nc.vector.tensor_copy(g["pair_lo"][:, :], table_ps[0:1, 32:32 + NT])
            link(nc.vector.tensor_copy(g["halves"][:, 0, :], table_ps[0:1, 64:64 + NG + 1]))
            link(nc.vector.tensor_copy(g["halves"][:, 1, 0:NG], table_ps[0:1, 164:164 + NG]))
            link(nc.vector.tensor_tensor(g["halves"][:, 1, 0:NG], g["halves"][:, 1, 0:NG],
                                         g["halves"][:, 0, 0:NG], ALU.add))
            nc.vector.tensor_copy(g["half_lo"][:, 0, :], table_ps[0:1, 264:264 + NG])
            link(nc.vector.tensor_copy(g["half_lo"][:, 1, :], table_ps[0:1, 364:364 + NG]))
            link(nc.vector.memset(g["counts"][:, :].rearrange("p (t w) -> p t w", w=CW)[:, :, N:CW], 0.0))
            link(nc.vector.tensor_scalar(src_f[:, :], src_i[:, :], -float(MID), None, ALU.add))
            nc.vector.tensor_scalar(dst_f[:, :], dst_i[:, :], -float(MID), None, ALU.add).then_inc(tables, 1)
            dve.wait_ge(tables, 1)
            with dve.Fori(0, NT) as j:
                begin = dve.value_load(g["pairs"][0:1, bass.ds(j, 1)], min_val=0, max_val=NT * NPAIR)
                end = dve.value_load(g["pairs"][0:1, bass.ds(j + 1, 1)], min_val=1, max_val=NT * NPAIR)
                lo = dve.value_load(g["pair_lo"][0:1, bass.ds(j, 1)], min_val=0, max_val=NPAIR - 1)
                with dve.Fori(begin, end) as s:
                    tile = within(nc, (s + lo - begin) * 2, ET - 2)
                    for i in range(2):
                        dve.wait_ge(used[i], s + 1)
                        nc.vector.tensor_scalar(pick[:, i, :], iota[:, bass.ds(j * NP, 128)],
                                                dst_f[:, bass.ds(tile + i, 1)], None, ALU.is_equal)
                        nc.vector.tensor_scalar(onehot[i], iota, src_f[:, bass.ds(tile + i, 1)], None,
                                                ALU.is_equal).then_inc(ready[i], 1)
            for b in range(7):
                dve.wait_ge(emptied[b], NT + 1)
            link(nc.vector.reduce_sum(g["indeg"][:, :], deg7[:, :, :], AX))
            normalize_relu(nc, link, root_asked, root_done, dve, g["x"][:, :, :], g["h"][:, :, :],
                           g["work32"][0:NP, 0:NT * D].rearrange("p (t d) -> p t d", d=D), g["s"], 1)

        @block.tensor
        def _(pe):
            pe.sem_inc(used[0], 1)
            pe.sem_inc(used[1], 1)
            for b in range(7):
                pe.sem_inc(emptied[b], 1)
            pe.wait_ge(made, 8)
            pe.wait_ge(parts, 1)
            nc.tensor.transpose(table_ps[0:NT, 0:NG], lo_part, ident[0:NG, 0:NG])
            nc.tensor.transpose(table_ps[0:NT, 128:128 + NG], hi_part, ident[0:NG, 0:NG]).then_inc(turned, 1)
            pe.wait_ge(spans, 1)

            def row(at, width, column, matrix):
                return nc.tensor.matmul(table_ps[0:1, at:at + width], column, matrix, start=True, stop=True)
            row(0, NT + 1, span[:, 1:2], before[0:NT, 0:NT + 1])
            row(32, NT, span[:, 0:1], ident[0:NT, 0:NT])
            row(64, NG + 1, jtotal, before[0:NG, 0:NG + 1])
            row(164, NG, jcount[:, 0:1], ident[0:NG, 0:NG])
            row(264, NG, jlo[:, 0:1], ident[0:NG, 0:NG])
            row(364, NG, jlo[:, 1:2], ident[0:NG, 0:NG]).then_inc(rows, 1)
            pe.wait_ge(tables, 1)
            with pe.Fori(0, NT) as j:
                begin = pe.value_load(g["pairs"][0:1, bass.ds(j, 1)], min_val=0, max_val=NT * NPAIR)
                end = pe.value_load(g["pairs"][0:1, bass.ds(j + 1, 1)], min_val=1, max_val=NT * NPAIR)
                for b in range(7):
                    pe.wait_ge(emptied[b], j + 1)
                    nc.tensor.matmul(sums[:, BANK * b:BANK * b + widths[b]], zeros[:, 0:128],
                                     zeros[:, 0:widths[b]], start=True, stop=True)
                with pe.Fori(begin, end) as s:
                    for i in range(2):
                        pe.wait_ge(ready[i], s + 1)
                        for b in range(7):
                            w = widths[b]
                            last = nc.tensor.matmul(sums[:, BANK * b:BANK * b + w], pick[:, i, :],
                                                    onehot[i][:, BANK * b:BANK * b + w], start=False, stop=True,
                                                    skip_group_check=True)
                        last.then_inc(used[i], 1)



def power_iterations(nc, g):
    with ExitStack() as ctx:
        m = Memory(nc, ctx, "hop")
        counts, x, h, t, s, indeg = (g[k] for k in ("counts", "x", "h", "t", "s", "indeg"))
        half = [g["work"][0:NP, NT * 2 * D * i:NT * 2 * D * (i + 1)].rearrange("p (t d) -> p t d", t=NT)
                for i in range(2)]
        ones = m.sb("ones", [NP, 1], F16)
        outdeg = m.sb("outdeg", [NP, NT], F32)
        degin = m.sb("degin", [NP, NT], F32)
        rc = m.sb("rc", [NP, NT], F32)
        gain = m.sb("gain", [NP, NT], F32)
        sums = m.ps("sums", [128, 8, BANK], F32)
        set_up = m.sem("set_up"); chain = m.sem("chain"); degrees = m.sem("degrees")
        root_asked = m.sem("root_asked"); root_done = m.sem("root_done")
        value = m.sem("value"); high = m.sem("high"); split = m.sem("split"); scaled = m.sem("scaled")
        summed = m.sem("summed"); drained = m.sem("drained")
        block = ctx.enter_context(nc.Block())
        ngr = len(GROUPS)

        @block.scalar
        def _(act):
            def square_root(nth):
                act.wait_ge(root_asked, nth)
                nc.scalar.activation(s[:, 2, :], s[:, 1, :], ACT.Sqrt).then_inc(root_done, 1)

            def highs(seen, to):
                for q, (m0, n) in enumerate(GROUPS):
                    act.wait_ge(value, seen + (q + 1))
                    nc.scalar.activation(half[to][:, m0:m0 + n, 0:D], t[:, m0:m0 + n, :],
                                         ACT.Copy).then_inc(high, 1)
            square_root(1)
            highs(0, 0)
            square_root(2)
            with act.Fori(0, HOPS // 2) as i:
                highs(i * (2 * ngr) + ngr, 1)
                highs(i * (2 * ngr) + 2 * ngr, 0)
            square_root(3)

        @block.vector
        def _(dve):
            link = Chain(dve, chain)
            nc.vector.memset(ones[:, :], 1.0).then_inc(set_up, 1)
            var, root, inv, tmp = (s[:, i, :] for i in range(1, 5))
            link(nc.vector.tensor_scalar(degin[:, :], indeg[:, :], 1.0, None, ALU.max))
            link(nc.vector.tensor_copy(var, degin[:, :]))
            inverse_root(nc, link, root_asked, root_done, dve, var, root, inv, tmp, 1)
            link(nc.vector.tensor_copy(rc[:, :], inv))
            link(nc.vector.tensor_scalar(tmp, rc[:, :], LIFT, None, ALU.mult))
            seen = 0
            for m0, n in GROUPS:
                nc.vector.tensor_tensor(t[:, m0:m0 + n, :], h[:, m0:m0 + n, :], spread(tmp[:, m0:m0 + n], D),
                                        ALU.mult).then_inc(value, 1)
            for q, (m0, n) in enumerate(GROUPS):
                dve.wait_ge(high, q + 1)
                nc.vector.tensor_tensor(half[0][:, m0:m0 + n, D:2 * D], t[:, m0:m0 + n, :],
                                        half[0][:, m0:m0 + n, 0:D], ALU.subtract).then_inc(split, 1)
            link(nc.vector.tensor_scalar(h[:, :, :], t[:, :, :], ALPHA, None, ALU.mult))
            dve.wait_ge(degrees, 1)
            link(nc.vector.tensor_copy(outdeg[:, :], sums[0:NP, 7, 0:NT]))
            link(nc.vector.tensor_scalar(var, outdeg[:, :], 1.0, None, ALU.max))
            inverse_root(nc, link, root_asked, root_done, dve, var, root, inv, tmp, 2)
            link(nc.vector.tensor_tensor(gain[:, :], inv, rc[:, :], ALU.mult))
            link(nc.vector.tensor_scalar(gain[:, :], gain[:, :], BETA, None, ALU.mult))
            dve.sem_inc(drained, 2)
            dve.wait_ge(drained, 2)

            def hop(done, to):
                for q, (m0, n) in enumerate(GROUPS):
                    g0 = 4 * ((q + to + 1) % 2)
                    v = t[:, m0:m0 + n, :]
                    dve.wait_ge(summed, done + (q + 1))
                    both = sums[0:NP, g0:g0 + n, 0:2 * D].rearrange("p n (a d) -> p n d a", a=2)
                    nc.vector.reduce_sum(v, both, AX).then_inc(drained, 1)
                    dve.wait_ge(drained, done + (q + 3))
                    nc.vector.tensor_tensor(v, v, spread(gain[:, m0:m0 + n], D), ALU.mult).then_inc(scaled, 1)
                    dve.wait_ge(scaled, done + (q + 1))
                    nc.vector.tensor_tensor(v, v, h[:, m0:m0 + n, :], ALU.add).then_inc(value, 1)
                    dve.wait_ge(high, done + (q + 1 + ngr))
                    nc.vector.tensor_tensor(half[to][:, m0:m0 + n, D:2 * D], v, half[to][:, m0:m0 + n, 0:D],
                                            ALU.subtract).then_inc(split, 1)
            with dve.Fori(0, HOPS // 2) as i:
                hop(i * (2 * ngr), 1)
                hop(i * (2 * ngr) + ngr, 0)
            link(nc.vector.tensor_tensor(tmp, degin[:, :], rc[:, :], ALU.mult))
            link(nc.vector.tensor_scalar(tmp, tmp, 1.0 / (THETA * LIFT), None, ALU.mult))
            link(nc.vector.tensor_tensor(t[:, :, :], t[:, :, :], spread(tmp, D), ALU.mult))
            link(nc.vector.tensor_tensor(x[:, :, :], x[:, :, :], t[:, :, :], ALU.add))
            normalize_relu(nc, link, root_asked, root_done, dve, x[:, :, :], h[:, :, :], t[:, :, :], s, 3)

        @block.tensor
        def _(pe):
            pe.wait_ge(set_up, 1)
            for m0 in range(NT):
                for k in range(NT):
                    last = nc.tensor.matmul(sums[:, 7, m0:m0 + 1], counts[0:NP, k * CW + m0 * NP:k * CW + m0 * NP + 128],
                                            ones[:, :], start=(k == 0), stop=(k == NT - 1))
            last.then_inc(degrees, 1)

            def hop(done, frm):
                for q, (m0, n) in enumerate(GROUPS):
                    g0 = 4 * ((q + frm) % 2)
                    pe.wait_ge(drained, done + (q + 1))
                    for i in range(n):
                        for k in range(NT):
                            if q == 0 and i == 0 and k % 4 == 0:
                                pe.wait_ge(split, done + (k // 4 + 1))
                            at = k * CW + (m0 + i) * NP
                            last = nc.tensor.matmul(sums[:, g0 + i, 0:2 * D], counts[0:NP, at:at + 128],
                                                    half[frm][:, k, :], start=(k == 0), stop=(k == NT - 1))
                    last.then_inc(summed, 1)
            with pe.Fori(0, HOPS // 2) as i:
                hop(i * (2 * ngr), 0)
                hop(i * (2 * ngr) + ngr, 1)


def transpose_counts(nc, g):
    with ExitStack() as ctx:
        m = Memory(nc, ctx, "turn")
        counts = g["counts"][0:NP, :].rearrange("p (t w) -> p t w", w=CW)
        ident = m.sb("ident", [NP, NP], F16)
        near = m.ps("near", [128, 4, 1024], F16)
        far = m.ps("far", [128, 4, 1024], F16)
        full = m.sem("full"); near_out = m.sem("near_out"); far_out = m.sem("far_out"); made = m.sem("made")
        chunks = [(a, b, min(4, NT - b)) for a in range(NT) for b in range(a + 1, NT, 4)]
        chunks += [(None, b, n) for b, n in GROUPS]
        block = ctx.enter_context(nc.Block())

        @block.vector
        def _(dve):
            nc.vector.tensor_copy(ident[:, :], g["ident"][0:NP, 0:NP]).then_inc(made, 1)
            for c, (a, b, n) in enumerate(chunks):
                dve.wait_ge(full, c + 1)
                got = near[0:NP, c % 4, 0:512].rearrange("p (n w) -> p n w", w=128)[:, 0:n, 0:NP]
                if a is None:
                    for i in range(n):
                        last = nc.vector.tensor_copy(counts[:, b + i, (b + i) * NP:(b + i + 1) * NP], got[:, i, :])
                else:
                    last = nc.vector.tensor_copy(counts[:, b:b + n, a * NP:(a + 1) * NP], got)
                last.then_inc(near_out, 1)

        @block.scalar
        def _(act):
            for c, (a, b, n) in enumerate(chunks):
                if a is not None:
                    act.wait_ge(full, c + 1)
                    got = far[0:NP, c % 4, 0:512].rearrange("p (n w) -> p n w", w=128)[:, 0:n, 0:NP]
                    to = counts[:, a, b * NP:(b + n) * NP].rearrange("p (n w) -> p n w", w=NP)
                    nc.scalar.activation(to, got, ACT.Copy).then_inc(far_out, 1)

        @block.tensor
        def _(pe):
            pe.wait_ge(made, 1)
            for c, (a, b, n) in enumerate(chunks):
                if c >= 4:
                    pe.wait_ge(near_out, c - 3)
                    pe.wait_ge(far_out, c - 3 if chunks[c - 4][0] is not None else far_chunks)
                if a is not None:
                    far_chunks = c + 1
                for i in range(n):
                    at = 128 * i
                    if a is None:
                        last = nc.tensor.transpose(near[0:NP, c % 4, at:at + NP],
                                                   counts[:, b + i, (b + i) * NP:(b + i + 1) * NP], ident[:, :])
                    else:
                        nc.tensor.transpose(near[0:NP, c % 4, at:at + NP],
                                            counts[:, a, (b + i) * NP:(b + i + 1) * NP], ident[:, :])
                        last = nc.tensor.transpose(far[0:NP, c % 4, at:at + NP],
                                                   counts[:, b + i, a * NP:(a + 1) * NP], ident[:, :])
                last.then_inc(full, 1)


def convolutions(nc, g, weights, biases):
    with ExitStack() as ctx:
        m = Memory(nc, ctx, "conv")
        counts, x, h, t, s, indeg = (g[k] for k in ("counts", "x", "h", "t", "s", "indeg"))
        parts = g["work"][0:NP, 0:NT * 3 * D].bitcast(BF16).rearrange("p (t d) -> p t d", t=NT)
        hT = g["work"][0:D, NT * 3 * D:NT * 3 * D + 2000].bitcast(F32).rearrange("p (i w) -> p i w", i=2)
        w_sb = m.sb("w", [D, 3, D], F32)
        b_sb = m.sb("b", [NP, 3, D], F32)
        sums = m.ps("sums", [128, 8, BANK], F32)
        loaded = m.sem("loaded"); chain = m.sem("chain")
        root_asked = m.sem("root_asked"); root_done = m.sem("root_done")
        turned = m.sem("turned"); turned_out = m.sem("turned_out"); mixed = m.sem("mixed")
        value = m.sem("value"); first = m.sem("first"); rest = m.sem("rest"); second = m.sem("second")
        split = m.sem("split"); summed = m.sem("summed"); drained = m.sem("drained"); passed = m.sem("passed")
        ngr = len(GROUPS)
        block = ctx.enter_context(nc.Block())

        @block.sync
        def _(sp):
            for i in range(3):
                sp.dma_start(w_sb[:, i, :], weights[i]).then_inc(loaded, 16)
                sp.dma_start(b_sb[:, i, :], biases[i].unsqueeze(0).to_broadcast([NP, D])).then_inc(loaded, 16)

        @block.scalar
        def _(act):
            def split_parts(k, m0, n):
                act.wait_ge(value, k + 1)
                nc.scalar.activation(parts[:, m0:m0 + n, 0:D], t[:, m0:m0 + n, :], ACT.Copy).then_inc(first, 1)
                act.wait_ge(rest, k + 1)
                nc.scalar.activation(parts[:, m0:m0 + n, D:2 * D], h[:, m0:m0 + n, :], ACT.Copy).then_inc(second, 1)

            act.wait_ge(root_asked, 1)
            nc.scalar.activation(s[:, 2, :], s[:, 1, :], ACT.Sqrt).then_inc(root_done, 1)
            for c in range(3):
                for q, (m0, n) in enumerate(GROUPS):
                    k = c * ngr + q
                    act.wait_ge(turned, k + 1)
                    nc.scalar.activation(hT[:, q % 2, 0:n * NP].rearrange("p (n w) -> p n w", w=NP),
                                         sums[0:D, q % 2, 0:n * 128].rearrange("p (n w) -> p n w", w=128)[:, :, 0:NP],
                                         ACT.Copy).then_inc(turned_out, 1)
                    if q >= 1:
                        split_parts(k - 1, *GROUPS[q - 1])
                split_parts((c + 1) * ngr - 1, *GROUPS[-1])
            act.wait_ge(root_asked, 2)
            nc.scalar.activation(s[:, 2, :], s[:, 1, :], ACT.Sqrt).then_inc(root_done, 1)

        @block.vector
        def _(dve):
            link = Chain(dve, chain)
            var, root, dinv, tmp = (s[:, i, :] for i in range(1, 5))
            link(nc.vector.tensor_scalar(var, indeg[:, :], 1.0, None, ALU.add))
            inverse_root(nc, link, root_asked, root_done, dve, var, root, dinv, tmp, 1)
            dve.wait_ge(loaded, 96)
            for c in range(3):
                for q, (m0, n) in enumerate(GROUPS):
                    k = c * ngr + q
                    dve.wait_ge(mixed, k + 1)
                    got = sums[0:NP, 2 + q % 2, 0:n * 128].rearrange("p (n w) -> p n w", w=128)[:, :, 0:D]
                    nc.vector.tensor_tensor(t[:, m0:m0 + n, :], got, spread(dinv[:, m0:m0 + n], D),
                                            ALU.mult).then_inc(value, 1)
                    dve.wait_ge(first, k + 1)
                    nc.vector.tensor_tensor(h[:, m0:m0 + n, :], t[:, m0:m0 + n, :], parts[:, m0:m0 + n, 0:D],
                                            ALU.subtract).then_inc(rest, 1)
                    dve.wait_ge(second, k + 1)
                    nc.vector.tensor_tensor(parts[:, m0:m0 + n, 2 * D:3 * D], h[:, m0:m0 + n, :],
                                            parts[:, m0:m0 + n, D:2 * D], ALU.subtract).then_inc(split, 1)
                for q, (m0, n) in enumerate(GROUPS):
                    k = c * ngr + q
                    v = h[:, m0:m0 + n, :]
                    dve.wait_ge(summed, k + 1)
                    three = sums[0:NP, 4 * (q % 2):4 * (q % 2) + n, 0:3 * D].rearrange("p n (a d) -> p n d a", a=3)
                    nc.vector.reduce_sum(v, three, AX).then_inc(drained, 1)
                    dve.wait_ge(drained, k + 1)
                    link(nc.vector.tensor_tensor(v, v, t[:, m0:m0 + n, :], ALU.add))
                    link(nc.vector.tensor_tensor(v, v, spread(dinv[:, m0:m0 + n], D), ALU.mult))
                    link(nc.vector.tensor_tensor(v, v, b_sb[:, c, :].unsqueeze(1).to_broadcast([NP, n, D]), ALU.add))
                    if c < 2:
                        nc.vector.tensor_scalar(v, v, 0.0, None, ALU.max).then_inc(passed, 1)
            link(nc.vector.tensor_tensor(x[:, :, :], x[:, :, :], h[:, :, :], ALU.add))
            normalize_relu(nc, link, root_asked, root_done, dve, x[:, :, :], h[:, :, :], t[:, :, :], s, 2)

        @block.tensor
        def _(pe):
            pe.wait_ge(loaded, 96)
            for c in range(3):
                def mix(q):
                    k = c * ngr + q
                    pe.wait_ge(turned_out, k + 1)
                    if q >= 2:
                        pe.wait_ge(value, k - 1)
                    for i in range(GROUPS[q][1]):
                        last = nc.tensor.matmul(sums[0:NP, 2 + q % 2, i * 128:i * 128 + D],
                                                hT[:, q % 2, i * NP:(i + 1) * NP], w_sb[:, c, :],
                                                start=True, stop=True)
                    last.then_inc(mixed, 1)
                if c:
                    pe.wait_ge(drained, c * ngr)
                for q, (m0, n) in enumerate(GROUPS):
                    k = c * ngr + q
                    if c:
                        pe.wait_ge(passed, (c - 1) * ngr + q + 1)
                    if q >= 2:
                        pe.wait_ge(turned_out, k - 1)
                    for i in range(n):
                        last = nc.tensor.transpose(sums[0:D, q % 2, i * 128:i * 128 + NP], h[:, m0 + i, :],
                                                   g["ident"][0:NP, 0:NP])
                    last.then_inc(turned, 1)
                    if q >= 1:
                        mix(q - 1)
                mix(ngr - 1)
                for q, (m0, n) in enumerate(GROUPS):
                    k = c * ngr + q
                    if q >= 2:
                        pe.wait_ge(drained, k - 1)
                    if q == 0:
                        pe.wait_ge(value, (c + 1) * ngr)
                    for i in range(n):
                        for j in range(NT):
                            if q == 0 and i == 0 and j % 4 == 0:
                                pe.wait_ge(split, c * ngr + j // 4 + 1)
                            at = j * CW + (m0 + i) * NP
                            last = nc.tensor.matmul(sums[:, 4 * (q % 2) + i, 0:3 * D], counts[0:NP, at:at + 128],
                                                    parts[:, j, :], start=(j == 0), stop=(j == NT - 1))
                    last.then_inc(summed, 1)



def edge_inputs(m, width):
    e = {}
    e["src_i"] = m.sb("src_i", [EP, ET], I32)
    e["dst_i"] = m.sb("dst_i", [EP, ET], I32)
    e["dst_f"] = m.sb("dst_f", [EP, ET], F32)
    e["iota"] = m.sb("iota", [EP, N], F32)
    e["slots"] = m.sb("slots", [EP, 2, GT], I32)
    e["rows"] = m.sb("rows", [EP, 2, GT, width], F32)
    e["onehot"] = m.sb("onehot", [EP, SUB, NP], F32)
    return e


def skewed(engine, *stages):
    lead, last = len(stages) - 1, NG // 2 - 1
    for step in range(lead):
        for k in range(step + 1):
            stages[k](0, step - k)
    with engine.Fori(0, last) as i:
        for u in range(4):
            for k, stage in enumerate(stages):
                stage(i, u + lead - k)
    for u in range(4):
        for k, stage in enumerate(stages):
            if u + lead - k < 4:
                stage(last, u + lead - k)


def part(v):
    half, sub = v // 2 % 2, v % 2
    return v // 4, half, sub, slice(SUB * sub, SUB * (sub + 1))


def gather_rows(nc, pool, e, table, rows_used, slot_ready, turn, rows_ready):
    with pool.Fori(0, NG // 2) as i:
        for half in range(2):
            pool.wait_ge(rows_used[half], i * 2 + 2)
            pool.sem_inc(turn, 1)
            nc.gpsimd.tensor_copy(e["slots"][:, half, :],
                                  e["src_i"][:, bass.ds(i * (2 * GT) + half * GT, GT)]).then_inc(slot_ready, 1)
            pool.wait_ge(slot_ready, i * 2 + (half + 1))
            pool.sem_inc(turn, 1)
            for k in range(GT):
                nc.gpsimd.indirect_dma_start(
                    out=e["rows"][:, half, k, :], out_offset=None, in_=table,
                    in_offset=bass.IndirectOffsetOnAxis(ap=e["slots"][:, half, k:k + 1], axis=0),
                ).then_inc(rows_ready[half][k // SUB], 16)


def half_bounds(engine, g, group, sub, lo=True):
    h, most = g["halves"], 2 * NG * NT
    flat = h[0:1, :, :].rearrange("p a b -> p (a b)")
    first = g["half_lo"][0:1, :, :].rearrange("p a b -> p (a b)")
    begin = engine.value_load(flat[:, bass.ds(group + sub * (NG + 1), 1)], min_val=0, max_val=most)
    end = engine.value_load(flat[:, bass.ds(group + (1 if sub else NG + 1), 1)], min_val=1, max_val=most)
    if not lo:
        return begin, end
    return begin, end, engine.value_load(first[:, bass.ds(group + sub * NG, 1)], min_val=0, max_val=NT - 1)


def message_layer(nc, g, src, dst, edges, w1, b1, w2, b2):
    with ExitStack() as ctx:
        m = Memory(nc, ctx, "msg")
        x, h, s = g["x"], g["h"], g["s"]
        e = edge_inputs(m, D)
        table = nc.dram_tensor("h_rows", [N, D], F32, kind="Internal").ap()
        edge = m.sb("edge", [EP, 2, GT, D], F32)
        passed = m.sb("passed", [EP, 4, SUB, D], F32)
        agg = m.sb("agg", [NP, NT, D], F32)
        t = m.sb("t", [NP, NT, D], F32)
        w1_sb = m.sb("w1", [D, D], F32)
        w2_sb = m.sb("w2", [D, D], F32)
        b1_sb = m.sb("b1", [D, 1], F32)
        b2_sb = m.sb("b2", [NP, D], F32)
        aT = m.sb("aT", [D, 2, 4 * NP], F32)
        hid = m.sb("hid", [D, 2, 4 * NP], F32)
        sums = m.ps("sums", [128, 8, BANK], F32)
        stored = m.sem("stored"); loaded = m.sem("loaded"); made = m.sem("made"); chain = m.sem("chain")
        rows_used = [m.sem(f"rows_used{i}") for i in range(2)]
        rows_ready = [[m.sem(f"rows_ready{i}{k}") for k in range(2)] for i in range(2)]
        edge_ready = [m.sem(f"edge_ready{i}") for i in range(2)]
        slot_ready = m.sem("slot_ready"); turn = m.sem("turn")
        added = m.sem("added"); sent = m.sem("sent"); half_done = m.sem("half_done")
        onehot_ready = m.sem("onehot_ready"); onehot_used = m.sem("onehot_used")
        tile_summed = m.sem("tile_summed"); tile_added = m.sem("tile_added"); ready = m.sem("ready")
        all_summed = m.sem("all_summed")
        turned = m.sem("turned"); turned_out = m.sem("turned_out"); hidden = m.sem("hidden")
        hidden_out = m.sem("hidden_out"); mixed = m.sem("mixed"); mixed_out = m.sem("mixed_out")
        root_asked = m.sem("root_asked"); root_done = m.sem("root_done")
        block = ctx.enter_context(nc.Block())

        @block.sync
        def _(sp):
            sp.dma_start(table.rearrange("(t p) d -> p t d", p=NP), h[:, :, :]).then_inc(stored, 16)
            sp.dma_start(e["src_i"][:, :], src).then_inc(loaded, 16)
            sp.dma_start(e["dst_i"][:, :], dst).then_inc(loaded, 16)
            sp.dma_start(w1_sb[:, :], w1).then_inc(loaded, 16)
            sp.dma_start(w2_sb[:, :], w2).then_inc(loaded, 16)
            sp.dma_start(b1_sb[:, :], b1.unsqueeze(1)).then_inc(loaded, 16)
            sp.dma_start(b2_sb[:, :], b2.unsqueeze(0).to_broadcast([NP, D])).then_inc(loaded, 16)
            with sp.Fori(0, NG // 2) as i:
                for half in range(2):
                    sp.wait_ge(rows_used[half], i * 2 + 2)
                    sp.dma_start(edge[:, half, :, :].rearrange("p k d -> p (k d)"),
                                 edges[bass.ds(i * 2 + half, 1), :, :].rearrange("a p d -> (a p) d"),
                                 ).then_inc(edge_ready[half], 16)

        @block.gpsimd
        def _(pool):
            nc.gpsimd.iota(e["iota"][:, :], [[1, N]], base=0, channel_multiplier=0,
                           allow_small_or_imprecise_dtypes=True).then_inc(made, 1)
            pool.wait_ge(loaded, 96)
            pool.wait_ge(stored, 16)
            gather_rows(nc, pool, e, table, rows_used, slot_ready, turn, rows_ready)

        @block.scalar
        def _(act):
            def send(i, v):
                turn_of, half, sub, tiles = part(v)
                act.wait_ge(added, i * 4 + (v + 1))
                act.wait_ge(half_done, i * 4 + (v + 1))
                nc.scalar.activation(passed[:, v % 4, :, :], e["rows"][:, half, tiles, :],
                                     ACT.Relu).then_inc(rows_used[half], 1)
                act.wait_ge(rows_used[half], i * 2 + (2 * turn_of + sub + 3))
                act.sem_inc(sent, 1)
            skewed(act, send)
            act.wait_ge(loaded, 96)
            for q, (m0, n) in enumerate(GROUPS):
                act.wait_ge(turned, q + 1)
                nc.scalar.activation(aT[:, q % 2, 0:n * NP].rearrange("p (n w) -> p n w", w=NP),
                                     sums[0:D, 2 * (q % 2), 0:n * 128].rearrange("p (n w) -> p n w", w=128)[:, :, 0:NP],
                                     ACT.Copy).then_inc(turned_out, 1)
                act.wait_ge(hidden, q + 1)
                nc.scalar.activation(hid[:, q % 2, 0:n * NP], sums[0:D, 2 * (q % 2) + 1, 0:n * NP], ACT.Relu,
                                     bias=b1_sb[:, 0:1]).then_inc(hidden_out, 1)
            act.wait_ge(root_asked, 1)
            nc.scalar.activation(s[:, 2, :], s[:, 1, :], ACT.Sqrt).then_inc(root_done, 1)

        @block.vector
        def _(dve):
            link = Chain(dve, chain)
            dve.wait_ge(loaded, 96)
            dve.wait_ge(made, 1)
            nc.vector.tensor_copy(agg[:, :, :], h[:, :, :])
            link(nc.vector.tensor_copy(e["dst_f"][:, :], e["dst_i"][:, :]))

            def add_edges(i, v):
                turn_of, half, sub, tiles = part(v)
                r = e["rows"][:, half, tiles, :]
                dve.wait_ge(edge_ready[half], i * 16 + 16 * (turn_of + 1))
                dve.wait_ge(rows_ready[half][sub], i * (16 * SUB) + 16 * SUB * (turn_of + 1))
                nc.vector.tensor_tensor(r, r, edge[:, half, tiles, :], ALU.add).then_inc(added, 1)

            def sum_messages(i, v):
                _, half, sub, _ = part(v)
                begin, end, lo = half_bounds(dve, g, i * 2 + half, sub)
                with dve.Fori(begin, end) as step:
                    j = within(nc, step + lo - begin, NT - 1)
                    for k in range(SUB):
                        dve.wait_ge(onehot_used, step * SUB + (k + 1))
                        nc.vector.tensor_scalar(
                            e["onehot"][:, k, :], e["iota"][:, bass.ds(j * NP, NP)],
                            e["dst_f"][:, bass.ds(i * (2 * GT) + (half * GT + SUB * sub + k), 1)],
                            None, ALU.is_equal).then_inc(onehot_ready, 1)
                    to = agg[:, bass.ds(j, 1), :].rearrange("p a d -> p (a d)")
                    dve.wait_ge(tile_summed, step + 1)
                    nc.vector.tensor_tensor(to, to, sums[0:NP, 0, 0:D], ALU.add).then_inc(tile_added, 1)
                    dve.wait_ge(tile_added, step + 2)
                    dve.sem_inc(ready, 1)
                dve.sem_inc(half_done, 1)
            skewed(dve, add_edges, sum_messages)
            dve.sem_inc(all_summed, 1)
            for q, (m0, n) in enumerate(GROUPS):
                v = t[:, m0:m0 + n, :]
                dve.wait_ge(mixed, q + 1)
                got = sums[0:NP, 4 + q % 2, 0:n * 128].rearrange("p (n w) -> p n w", w=128)[:, :, 0:D]
                nc.vector.tensor_tensor(v, got, b2_sb[:, :].unsqueeze(1).to_broadcast([NP, n, D]),
                                        ALU.add).then_inc(mixed_out, 1)
                dve.wait_ge(mixed_out, q + 1)
                link(nc.vector.scalar_tensor_tensor(out=v, in0=v, scalar=0.0, in1=h[:, m0:m0 + n, :],
                                                    op0=ALU.max, op1=ALU.add))
                link(nc.vector.tensor_tensor(x[:, m0:m0 + n, :], x[:, m0:m0 + n, :], v, ALU.add))
            normalize_relu(nc, link, root_asked, root_done, dve, x[:, :, :], h[:, :, :], t[:, :, :], s, 1)

        @block.tensor
        def _(pe):
            for i in range(2):
                pe.sem_inc(rows_used[i], 2)
            pe.sem_inc(half_done, 4)
            pe.sem_inc(onehot_used, SUB)
            pe.sem_inc(tile_added, 1)
            with pe.Fori(0, NG // 2) as i:
                for half in range(2):
                    for sub in range(2):
                        u = 2 * half + sub
                        begin, end = half_bounds(pe, g, i * 2 + half, sub, lo=False)
                        with pe.Fori(begin, end) as step:
                            pe.wait_ge(sent, i * 4 + (u + 1))
                            pe.wait_ge(tile_added, step + 1)
                            for k in range(SUB):
                                pe.wait_ge(onehot_ready, step * SUB + (k + 1))
                                last = nc.tensor.matmul(sums[0:NP, 0, 0:D], e["onehot"][:, k, :],
                                                        passed[:, u, k, :], start=(k == 0), stop=(k == SUB - 1))
                                last.then_inc(onehot_used, 1)
                            pe.wait_ge(onehot_used, step * SUB + 2 * SUB)
                            pe.sem_inc(tile_summed, 1)
            pe.wait_ge(all_summed, 1)
            for q, (m0, n) in enumerate(GROUPS):
                if q >= 2:
                    pe.wait_ge(turned_out, q - 1)
                for i in range(n):
                    last = nc.tensor.transpose(sums[0:D, 2 * (q % 2), i * 128:i * 128 + NP], agg[:, m0 + i, :],
                                               g["ident"][0:NP, 0:NP])
                last.then_inc(turned, 1)
                pe.wait_ge(turned_out, q + 1)
                if q >= 2:
                    pe.wait_ge(hidden_out, q - 1)
                nc.tensor.matmul(sums[0:D, 2 * (q % 2) + 1, 0:n * NP], w1_sb[:, :], aT[:, q % 2, 0:n * NP],
                                 start=True, stop=True).then_inc(hidden, 1)
                pe.wait_ge(hidden_out, q + 1)
                if q >= 2:
                    pe.wait_ge(mixed_out, q - 1)
                for i in range(n):
                    last = nc.tensor.matmul(sums[0:NP, 4 + q % 2, i * 128:i * 128 + D],
                                            hid[:, q % 2, i * NP:(i + 1) * NP], w2_sb[:, :], start=True, stop=True)
                last.then_inc(mixed, 1)



def gated_layer(nc, g, src, dst, edges_T, mw1, mb1, mw2, mb2, gw1, gb1, gw2, gb2, uw1, ub1, uw2, ub2, ln_g, ln_b, out):
    with ExitStack() as ctx:
        m = Memory(nc, ctx, "gate")
        x, h, s = g["x"], g["h"], g["s"]
        e = edge_inputs(m, 2 * D)
        table = nc.dram_tensor("first_rows", [N, 2 * D], F32, kind="Internal").ap()
        edge = m.sb("edge", [DE, 2, GT * EP], F32)
        passed = m.sb("passed", [EP, 4, SUB, D + 1], F32)
        gated = m.sb("gated", [EP, 2, SUB, D], F32)
        gate = m.sb("gate", [EP, 2, SUB], F32)
        agg = m.sb("agg", [NP, NT, D + 1], F32)
        first = m.sb("first", [NP, 2, 4, 2 * D], F32)
        hT = m.sb("hT", [D, N], F32)
        wh = m.sb("wh", [D, 2 * D], F32)
        we = m.sb("we", [DE, 2 * D], F32)
        b1_sb = m.sb("b1", [NP, 2 * D], F32)
        gw2_sb = m.sb("gw2", [EP, D], F32)
        gb2_sb = m.sb("gb2", [EP, 1], F32)
        mw2_sb = m.sb("mw2", [D + 1, D], F32)
        uh = m.sb("uh", [D, D], F32)
        ua = m.sb("ua", [D, D], F32)
        ub1_sb = m.sb("ub1", [D, 1], F32)
        uw2_sb = m.sb("uw2", [D, D], F32)
        ub2_sb = m.sb("ub2", [NP, D], F32)
        scale_sb = m.sb("scale", [NP, D], F32)
        shift_sb = m.sb("shift", [NP, D], F32)
        aT = m.sb("aT", [D + 1, 4 * NP], F32)
        mT = m.sb("mT", [D, 4 * NP], F32)
        hid = m.sb("hid", [D, 4 * NP], F32)
        t = m.sb("t", [NP, NT, D], F32)
        sums = m.ps("sums", [128, 8, BANK], F32)
        stored = m.sem("stored"); loaded = m.sem("loaded"); made = m.sem("made"); chain = m.sem("chain")
        hT_ready = m.sem("hT_ready"); hT_out = m.sem("hT_out")
        first_ready = m.sem("first_ready"); first_out = m.sem("first_out")
        first_stored = [m.sem(f"first_stored{i}") for i in range(2)]
        rows_used = [m.sem(f"rows_used{i}") for i in range(2)]
        rows_ready = [[m.sem(f"rows_ready{i}{k}") for k in range(2)] for i in range(2)]
        edge_ready = [m.sem(f"edge_ready{i}") for i in range(2)]
        slot_ready = m.sem("slot_ready"); turn = m.sem("turn")
        edge_mixed = m.sem("edge_mixed"); added = m.sem("added"); freed = m.sem("freed"); sent = m.sem("sent")
        gate_in = m.sem("gate_in"); gate_sum = m.sem("gate_sum"); gate_out = m.sem("gate_out")
        half_done = m.sem("half_done")
        onehot_ready = m.sem("onehot_ready"); onehot_used = m.sem("onehot_used")
        tile_summed = m.sem("tile_summed"); tile_added = m.sem("tile_added"); ready = m.sem("ready")
        all_summed = m.sem("all_summed"); step_out = m.sem("step_out")
        turned = m.sem("turned"); second = m.sem("second"); hidden = m.sem("hidden"); mixed = m.sem("mixed")
        turned_out = m.sem("turned_out"); second_out = m.sem("second_out")
        hidden_out = m.sem("hidden_out"); mixed_out = m.sem("mixed_out")
        root_asked = m.sem("root_asked"); root_done = m.sem("root_done"); written = m.sem("written")
        block = ctx.enter_context(nc.Block())

        @block.sync
        def _(sp):
            row = lambda v, n: v.unsqueeze(0).to_broadcast([n, v.shape[0]])
            loads = [(e["src_i"][:, :], src), (e["dst_i"][:, :], dst),
                     (wh[:, 0:D], mw1[0:D, :]), (wh[:, D:2 * D], gw1[0:D, :]),
                     (we[:, 0:D], mw1[D:D + DE, :]), (we[:, D:2 * D], gw1[D:D + DE, :]),
                     (b1_sb[:, 0:D], row(mb1, NP)), (b1_sb[:, D:2 * D], row(gb1, NP)),
                     (gw2_sb[:, :], row(gw2.rearrange("d a -> (d a)"), EP)), (gb2_sb[:, :], row(gb2, EP)),
                     (mw2_sb[0:D, :], mw2), (mw2_sb[D:D + 1, :], row(mb2, 1)),
                     (uh[:, :], uw1[0:D, :]), (ua[:, :], uw1[D:2 * D, :]), (ub1_sb[:, :], ub1.unsqueeze(1)),
                     (uw2_sb[:, :], uw2), (ub2_sb[:, :], row(ub2, NP)),
                     (scale_sb[:, :], row(ln_g, NP)), (shift_sb[:, :], row(ln_b, NP))]
            assert len(loads) == LOADS
            for to, frm in loads:
                sp.dma_start(to, frm).then_inc(loaded, 16)
            tiles = table.rearrange("(t p) d -> p t d", p=NP)
            for q, (m0, n) in enumerate(GROUPS):
                sp.wait_ge(first_out, q + 1)
                sp.dma_start(tiles[:, m0:m0 + n, :], first[:, q % 2, 0:n, :]).then_inc(first_stored[q % 2], 16)
            with sp.Fori(0, NG // 2) as i:
                for half in range(2):
                    sp.wait_ge(rows_used[half], i * 2 + 2)
                    sp.dma_start(edge[:, half, :],
                                 edges_T[bass.ds(i * 2 + half, 1), :, :].rearrange("a p d -> (a p) d"),
                                 ).then_inc(edge_ready[half], 16)
            sp.wait_ge(written, 1)
            sp.dma_start(out.rearrange("(t p) d -> p t d", p=NP), x[:, :, :]).then_inc(stored, 16)
            sp.wait_ge(stored, 16)

        @block.gpsimd
        def _(pool):
            nc.gpsimd.iota(e["iota"][:, :], [[1, N]], base=0, channel_multiplier=0,
                           allow_small_or_imprecise_dtypes=True).then_inc(made, 1)
            nc.gpsimd.memset(agg[:, :, :], 0.0).then_inc(made, 1)
            nc.gpsimd.memset(passed[:, :, :, D:D + 1], 1.0).then_inc(made, 1)
            pool.wait_ge(loaded, 16 * LOADS)
            for i in range(2):
                pool.wait_ge(first_stored[i], 16 * ((len(GROUPS) + 1 - i) // 2))
            gather_rows(nc, pool, e, table, rows_used, slot_ready, turn, rows_ready)

        @block.scalar
        def _(act):
            for q, (m0, n) in enumerate(GROUPS):
                act.wait_ge(hT_ready, q + 1)
                nc.scalar.activation(hT[:, m0 * NP:(m0 + n) * NP].rearrange("p (n w) -> p n w", w=NP),
                                     sums[0:D, q % 2, 0:n * 128].rearrange("p (n w) -> p n w", w=128)[:, :, 0:NP],
                                     ACT.Copy).then_inc(hT_out, 1)

            def activate(i, v):
                turn_of, half, sub, tiles = part(v)
                r = e["rows"][:, half, tiles, :]
                act.wait_ge(added, i * 4 + (v + 1))
                act.sem_inc(freed, 1)
                act.wait_ge(gate_sum, i * 4 + (v + 2))
                nc.scalar.activation(gated[:, v % 2, :, :], r[:, :, D:2 * D], ACT.Gelu).then_inc(gate_in, 1)
                act.wait_ge(half_done, i * 4 + (v + 1))
                nc.scalar.activation(passed[:, v % 4, :, 0:D], r[:, :, 0:D], ACT.Gelu).then_inc(rows_used[half], 1)
                act.wait_ge(rows_used[half], i * 2 + (2 * turn_of + sub + 3))
                act.sem_inc(sent, 1)

            def open_gates(i, v):
                act.wait_ge(gate_sum, i * 4 + (v + 4))
                nc.scalar.activation(gate[:, v % 2, :], gate[:, v % 2, :], ACT.Tanh, scale=0.5,
                                     bias=gb2_sb[:, 0:1]).then_inc(gate_out, 1)
            skewed(act, activate, open_gates)
            for q, (m0, n) in enumerate(GROUPS):
                act.wait_ge(turned, q + 1)
                nc.scalar.activation(aT[:, 0:n * NP].rearrange("p (n w) -> p n w", w=NP),
                                     sums[0:D + 1, 0, 0:n * 128].rearrange("p (n w) -> p n w", w=128)[:, :, 0:NP],
                                     ACT.Copy).then_inc(turned_out, 1)
                act.wait_ge(second, q + 1)
                nc.scalar.activation(mT[:, 0:n * NP], sums[0:D, 1, 0:n * NP], ACT.Copy).then_inc(second_out, 1)
                act.wait_ge(hidden, q + 1)
                nc.scalar.activation(hid[:, 0:n * NP], sums[0:D, 2, 0:n * NP], ACT.Gelu,
                                     bias=ub1_sb[:, 0:1]).then_inc(hidden_out, 1)
            act.wait_ge(root_asked, 1)
            nc.scalar.activation(s[:, 2, :], s[:, 1, :], ACT.Sqrt).then_inc(root_done, 1)

        @block.vector
        def _(dve):
            link = Chain(dve, chain)
            dve.wait_ge(loaded, 16 * LOADS)
            dve.wait_ge(made, 3)
            link(nc.vector.tensor_scalar(gb2_sb[:, :], gb2_sb[:, :], 0.5, None, ALU.mult))
            link(nc.vector.tensor_copy(e["dst_f"][:, :], e["dst_i"][:, :]))
            for q, (m0, n) in enumerate(GROUPS):
                dve.wait_ge(first_ready, q + 1)
                if q >= 2:
                    dve.wait_ge(first_stored[q % 2], 16 * (q // 2))
                got = sums[0:NP, 2 + 2 * (q % 2):4 + 2 * (q % 2), :].rearrange("p b (a d) -> p (b a) d", d=256)
                nc.vector.tensor_tensor(first[:, q % 2, 0:n, :], got[:, 0:n, 0:2 * D],
                                        b1_sb[:, :].unsqueeze(1).to_broadcast([NP, n, 2 * D]),
                                        ALU.add).then_inc(first_out, 1)

            def add_edges(i, v):
                turn_of, half, sub, tiles = part(v)
                r = e["rows"][:, half, tiles, :]
                products = sums[:, 2 * (v % 2):2 * (v % 2) + 2, :].rearrange("p b (a d) -> p (b a) d", d=256)
                dve.wait_ge(edge_mixed, i * 4 + (v + 1))
                dve.wait_ge(rows_ready[half][sub], i * (16 * SUB) + 16 * SUB * (turn_of + 1))
                nc.vector.tensor_tensor(r, r, products[:, :, 0:2 * D], ALU.add).then_inc(added, 1)

            def sum_gates(i, v):
                values = gated[:, v % 2, :, :]
                dve.wait_ge(gate_in, i * 4 + (v + 1))
                nc.vector.tensor_tensor(values, values, gw2_sb[:, :].unsqueeze(1).to_broadcast([EP, SUB, D]),
                                        ALU.mult).then_inc(ready, 1)
                dve.wait_ge(ready, i * 4 + (v + 1))
                nc.vector.reduce_sum(gate[:, v % 2, :], values, AX).then_inc(gate_sum, 1)

            def sum_messages(i, v):
                _, half, sub, _ = part(v)
                dve.wait_ge(gate_out, i * 4 + (v + 1))
                nc.vector.tensor_scalar(gate[:, v % 2, :], gate[:, v % 2, :], 0.5, 0.5, ALU.mult,
                                        ALU.add).then_inc(step_out, 1)
                begin, end, lo = half_bounds(dve, g, i * 2 + half, sub)
                with dve.Fori(begin, end) as step:
                    j = within(nc, step + lo - begin, NT - 1)
                    dve.wait_ge(step_out, i * 4 + (v + 1))
                    for k in range(SUB):
                        dve.wait_ge(onehot_used, step * SUB + (k + 1))
                        nc.vector.tensor_scalar(
                            e["onehot"][:, k, :], e["iota"][:, bass.ds(j * NP, NP)],
                            e["dst_f"][:, bass.ds(i * (2 * GT) + (half * GT + SUB * sub + k), 1)],
                            gate[:, v % 2, k:k + 1], ALU.is_equal, ALU.mult).then_inc(onehot_ready, 1)
                    to = agg[:, bass.ds(j, 1), :].rearrange("p a d -> p (a d)")
                    dve.wait_ge(tile_summed, step + 1)
                    nc.vector.tensor_tensor(to, to, sums[0:NP, 4, 0:D + 1], ALU.add).then_inc(tile_added, 1)
                    dve.wait_ge(tile_added, step + 2)
                    dve.sem_inc(all_summed, 1)
                dve.sem_inc(half_done, 1)
            skewed(dve, add_edges, sum_gates, sum_messages)
            for q, (m0, n) in enumerate(GROUPS):
                v = t[:, m0:m0 + n, :]
                dve.wait_ge(mixed, q + 1)
                got = sums[0:NP, 3, 0:n * 128].rearrange("p (n w) -> p n w", w=128)[:, :, 0:D]
                nc.vector.tensor_tensor(v, got, ub2_sb[:, :].unsqueeze(1).to_broadcast([NP, n, D]),
                                        ALU.add).then_inc(mixed_out, 1)
                dve.wait_ge(mixed_out, q + 1)
                link(nc.vector.tensor_tensor(v, v, h[:, m0:m0 + n, :], ALU.add))
            square = agg[:, :, :].rearrange("p t d -> p (t d)")[:, 0:NT * D].rearrange("p (t d) -> p t d", d=D)
            normalize_relu(nc, link, root_asked, root_done, dve, t[:, :, :], h[:, :, :], square, s, 1, relu=False)
            wide = [NP, NT, D]
            link(nc.vector.tensor_tensor(h[:, :, :], h[:, :, :], scale_sb[:, :].unsqueeze(1).to_broadcast(wide), ALU.mult))
            link(nc.vector.tensor_tensor(h[:, :, :], h[:, :, :], shift_sb[:, :].unsqueeze(1).to_broadcast(wide), ALU.add))
            nc.vector.tensor_tensor(x[:, :, :], x[:, :, :], h[:, :, :], ALU.add).then_inc(written, 1)

        @block.tensor
        def _(pe):
            for i in range(2):
                pe.sem_inc(rows_used[i], 2)
            pe.sem_inc(half_done, 4)
            pe.sem_inc(onehot_used, SUB)
            pe.sem_inc(tile_added, 1)
            pe.sem_inc(gate_sum, 3)
            pe.sem_inc(freed, 2)
            pe.wait_ge(loaded, 16 * LOADS)

            def first_rows(q):
                m0, n = GROUPS[q]
                pe.wait_ge(hT_out, q + 1)
                if q >= 2:
                    pe.wait_ge(first_out, q - 1)
                for i in range(n):
                    last = nc.tensor.matmul(sums[0:NP, 2 + 2 * (q % 2) + i // 2, 256 * (i % 2):256 * (i % 2) + 2 * D],
                                            hT[:, (m0 + i) * NP:(m0 + i + 1) * NP], wh[:, :], start=True, stop=True)
                last.then_inc(first_ready, 1)
            for q, (m0, n) in enumerate(GROUPS):
                if q >= 2:
                    pe.wait_ge(hT_out, q - 1)
                for i in range(n):
                    last = nc.tensor.transpose(sums[0:D, q % 2, i * 128:i * 128 + NP], h[:, m0 + i, :],
                                               g["ident"][0:NP, 0:NP])
                last.then_inc(hT_ready, 1)
                if q:
                    first_rows(q - 1)
            first_rows(len(GROUPS) - 1)
            pe.wait_ge(first_out, len(GROUPS))

            def mix_edges(i, v):
                turn_of, half, sub, _ = part(v)
                pe.wait_ge(edge_ready[half], i * 16 + 16 * (turn_of + 1))
                pe.wait_ge(freed, i * 4 + (v + 1))
                for k in range(SUB):
                    at = (SUB * sub + k) * EP
                    last = nc.tensor.matmul(sums[:, 2 * (v % 2) + k // 2, 256 * (k % 2):256 * (k % 2) + 2 * D],
                                            edge[:, half, at:at + EP], we[:, :], start=True, stop=True)
                last.then_inc(edge_mixed, 1)

            def wait_turn(i, v):
                pass

            def sum_messages(i, v):
                _, half, sub, _ = part(v)
                begin, end = half_bounds(pe, g, i * 2 + half, sub, lo=False)
                with pe.Fori(begin, end) as step:
                    pe.wait_ge(sent, i * 4 + (v + 1))
                    pe.wait_ge(tile_added, step + 1)
                    for k in range(SUB):
                        pe.wait_ge(onehot_ready, step * SUB + (k + 1))
                        last = nc.tensor.matmul(sums[0:NP, 4, 0:D + 1], e["onehot"][:, k, :],
                                                passed[:, v % 4, k, :], start=(k == 0), stop=(k == SUB - 1))
                        last.then_inc(onehot_used, 1)
                    pe.wait_ge(onehot_used, step * SUB + 2 * SUB)
                    pe.sem_inc(tile_summed, 1)
            skewed(pe, mix_edges, wait_turn, sum_messages)
            pe.wait_ge(half_done, 2 * NG + 4)
            for q, (m0, n) in enumerate(GROUPS):
                for i in range(n):
                    last = nc.tensor.transpose(sums[0:D + 1, 0, i * 128:i * 128 + NP], agg[:, m0 + i, :],
                                               g["ident"][0:NP, 0:NP])
                last.then_inc(turned, 1)
                pe.wait_ge(turned_out, q + 1)
                nc.tensor.matmul(sums[0:D, 1, 0:n * NP], mw2_sb[:, :], aT[:, 0:n * NP],
                                 start=True, stop=True).then_inc(second, 1)
                pe.wait_ge(second_out, q + 1)
                nc.tensor.matmul(sums[0:D, 2, 0:n * NP], uh[:, :], hT[:, m0 * NP:(m0 + n) * NP],
                                 start=True, stop=False)
                nc.tensor.matmul(sums[0:D, 2, 0:n * NP], ua[:, :], mT[:, 0:n * NP],
                                 start=False, stop=True).then_inc(hidden, 1)
                pe.wait_ge(hidden_out, q + 1)
                if q:
                    pe.wait_ge(mixed_out, q)
                for i in range(n):
                    last = nc.tensor.matmul(sums[0:NP, 3, i * 128:i * 128 + D], hid[:, i * NP:(i + 1) * NP],
                                            uw2_sb[:, :], start=True, stop=True)
                last.then_inc(mixed, 1)


def build(nc, x, src, dst, dst_groups, weights, biases, edges_96, edges_32, l2, l3, out, probe=None):
    with ExitStack() as ctx:
        m = Memory(nc, ctx, "all")
        g = {}
        g["x"] = m.sb("x", [NP, NT, D], F32)
        g["h"] = m.sb("h", [NP, NT, D], F32)
        g["s"] = m.sb("s", [NP, 5, NT], F32)
        g["ident"] = m.sb("ident", [128, 128], F32)
        g["halves"] = m.sb("halves", [1, 2, NG + 1], I32)
        g["half_lo"] = m.sb("half_lo", [1, 2, NG], I32)
        with ExitStack() as dense:
            m = Memory(nc, dense, "dense")
            g["counts"] = m.sb("counts", [128, NT * CW], F16)
            g["work"] = m.sb("work", [128, 2 * NT * 2 * D], F16)
            g["work32"] = g["work"][:, :].bitcast(F32)
            g["indeg"] = m.sb("indeg", [NP, NT], F32)
            g["pairs"] = m.sb("pairs", [1, NT + 1], I32)
            g["pair_lo"] = m.sb("pair_lo", [1, NT], I32)
            count_edges(nc, g, x, src, dst, dst_groups)
            if probe: probe(nc, g, 0)
            with nc.sbuf_tensor("dense_t", [NP, NT, D], F32) as t:
                g["t"] = t
                power_iterations(nc, g)
                if probe: probe(nc, g, 1)
                transpose_counts(nc, g)
                convolutions(nc, g, weights, biases)
                if probe: probe(nc, g, 2)
        message_layer(nc, g, src, dst, edges_96, *l2)
        if probe: probe(nc, g, 3)
        gated_layer(nc, g, src, dst, edges_32, *l3, out)


_L1 = [f"L1_gnn_{k}{i}" for k in "Wb" for i in (1, 2, 3)]
_L2 = [f"L2_gnn_{k}" for k in ("W1", "b1", "W2", "b2")]
_L3 = [f"L3_gnn_{k}" for k in ("mW1", "mb1", "mW2", "mb2", "gW1", "gb1", "gW2", "gb2",
                               "uW1", "ub1", "uW2", "ub2", "ln_g", "ln_b")]


def kernel(**inputs):
    import numpy as np
    import concourse.bacc as bacc
    from concourse.bass_utils import run_bass_kernel_spmd

    def padded(a, fill):
        a = np.asarray(a)
        return np.concatenate([a, np.full((NG * GT * EP - E,) + a.shape[1:], fill, a.dtype)])

    src, dst = padded(inputs["src"], 0), padded(inputs["dst"], N)
    arrays = {
        "x": np.asarray(inputs["x"]),
        "src": np.ascontiguousarray(src.reshape(ET, EP).T),
        "dst": np.ascontiguousarray(dst.reshape(ET, EP).T),
        "dst_groups": dst.reshape(NG, GT * EP),
        "edges_96": np.ascontiguousarray(padded(inputs["edge_attr_96"], 0).reshape(NG, GT, EP, D)
                                         .transpose(0, 2, 1, 3)).reshape(NG, EP, GT * D),
        "edges_32": np.ascontiguousarray(padded(inputs["edge_attr_32"], 0).reshape(NG, GT * EP, DE)
                                         .transpose(0, 2, 1)),
    }
    for name in _L1 + _L2 + _L3:
        arrays[name] = np.asarray(inputs[name])
    nc = bacc.Bacc("TRN2", target_bir_lowering=False, num_devices=1)
    t = {name: nc.dram_tensor(name, a.shape, mybir.dt.from_np(a.dtype), kind="ExternalInput").ap()
         for name, a in arrays.items()}
    out = nc.dram_tensor("out", (N, D), F32, kind="ExternalOutput").ap()
    build(nc, t["x"], t["src"], t["dst"], t["dst_groups"], [t[k] for k in _L1[:3]], [t[k] for k in _L1[3:]],
          t["edges_96"], t["edges_32"], [t[k] for k in _L2], [t[k] for k in _L3], out)
    result = run_bass_kernel_spmd(nc, [arrays], core_ids=[0])
    return result.results[0]["out"]
```
